# Optimizing a Trainium2 kernel written in Bass

```python
import numpy as np
import jax
import jax.numpy as jnp

def _softmax(x, axis=-1):
    return jax.nn.softmax(x, axis=axis)

def _gelu(x):
    return jax.nn.gelu(x, approximate=True)

def _silu(x):
    return jax.nn.silu(x)

def _sigmoid(x):
    return jax.nn.sigmoid(x)

def _layernorm(x, axis=-1, eps=1e-05):
    m = jnp.mean(x, axis=axis, keepdims=True)
    v = jnp.var(x, axis=axis, keepdims=True)
    return (x - m) / jnp.sqrt(v + eps)

def _scatter_add(tgt, idx, src, axis=0):
    return tgt.at[idx].add(src)

def _segment_sum(src, seg, n):
    return jax.ops.segment_sum(src, seg, n)
kernel_name = 'mk_adj_resnorm_d2_adj_r2_34768e'

def setup_inputs(seed: int=0):
    np.random.seed(seed)
    _w = jnp.asarray

    def _rec_inputs():
        import jax
        import jax.numpy as jnp
        _gk = jax.random.key(seed)
        x = -0.0003929 + 0.9999 * jax.random.normal(jax.random.fold_in(_gk, 1), (16, 512, 256), jnp.float32)
        _w = (1.0 + jnp.arange(512, dtype=jnp.float32)) ** (-0.5)
        _w = _w / _w.mean()
        _pij = jnp.clip(0.00390625 * _w[:, None] * _w[None, :], 0.0, 1.0)
        _a = jax.random.uniform(jax.random.fold_in(_gk, 2), (16, 512, 512)) < _pij
        _a = jnp.logical_or(_a, jnp.eye(512, dtype=bool))
        _af = _a.astype(jnp.float32)
        _af = _af * jax.random.uniform(jax.random.fold_in(_gk, 3), (16, 512, 512), jnp.float32, 0.05, 1)
        adj = _af
        return (x, adj)
    x, adj = _rec_inputs()

    def _L0_gnn_setup():
        import jax, jax.numpy as jnp
        import numpy as np
        B, N, C_IN, C_OUT = (8, 2048, 256, 256)
        key = jax.random.key(seed)
        k1, k2, k3, k4 = jax.random.split(key, 4)
        node_features = jax.random.normal(k1, (B, N, C_IN), dtype=jnp.float32)
        adj_matrix = jax.random.uniform(k2, (B, N, N), dtype=jnp.float32)
        W = jax.random.normal(k3, (C_IN, C_OUT), dtype=jnp.float32) / np.sqrt(C_IN)
        b = jax.random.normal(k4, (C_OUT,), dtype=jnp.float32) * 0.01
        return {'node_features': node_features, 'adj_matrix': adj_matrix, 'W': W, 'b': b}
    _L0_gnn_all = _L0_gnn_setup()
    _L0_gnn_in = {k: v for k, v in _L0_gnn_all.items() if k in ('W', 'b')}
    del _L0_gnn_all

    def _L1_gnn_setup():
        import jax, jax.numpy as jnp
        import numpy as np
        B, N, F_IN, F_HID, F_OUT = (32, 512, 256, 256, 256)

        def _gcn_layer(x, adj, W, b):
            support = jnp.einsum('bnf,fh->bnh', x, W)
            return jnp.einsum('bnm,bmh->bnh', adj, support) + b
        key = jax.random.key(seed)
        ks = jax.random.split(key, 8)

        def xavier(k, fan_in, fan_out):
            bound = float(np.sqrt(6.0 / (fan_in + fan_out)))
            return jax.random.uniform(k, (fan_in, fan_out), jnp.float32, -bound, bound)
        return {'batch_graph': jax.random.normal(ks[0], (B, N, F_IN), jnp.float32), 'adj': jax.random.uniform(ks[1], (B, N, N), jnp.float32), 'W1': xavier(ks[2], F_IN, F_HID), 'b1': jnp.zeros((F_HID,), jnp.float32), 'W2': xavier(ks[3], F_HID, F_HID), 'b2': jnp.zeros((F_HID,), jnp.float32), 'W3': xavier(ks[4], F_HID, F_OUT), 'b3': jnp.zeros((F_OUT,), jnp.float32)}
    _L1_gnn_all = _L1_gnn_setup()
    _L1_gnn_in = {k: v for k, v in _L1_gnn_all.items() if k in ('W1', 'b1', 'W2', 'b2', 'W3', 'b3')}
    del _L1_gnn_all
    return {'x': x, 'adj': adj, 'L0_gnn_W': _L0_gnn_in['W'], 'L0_gnn_b': _L0_gnn_in['b'], 'L1_gnn_W1': _L1_gnn_in['W1'], 'L1_gnn_b1': _L1_gnn_in['b1'], 'L1_gnn_W2': _L1_gnn_in['W2'], 'L1_gnn_b2': _L1_gnn_in['b2'], 'L1_gnn_W3': _L1_gnn_in['W3'], 'L1_gnn_b3': _L1_gnn_in['b3']}

def reference(x, adj, L0_gnn_W, L0_gnn_b, L1_gnn_W1, L1_gnn_b1, L1_gnn_W2, L1_gnn_b2, L1_gnn_W3, L1_gnn_b3):
    import jax
    import jax.numpy as jnp

    def _L0_gnn_ref(node_features, adj_matrix, W, b):
        import jax, jax.numpy as jnp
        import numpy as np
        B, N, C_IN, C_OUT = (8, 2048, 256, 256)
        num_neighbours = adj_matrix.sum(axis=-1, keepdims=True)
        h = jnp.einsum('bni,io->bno', node_features, W) + b
        h = jnp.einsum('bnm,bmo->bno', adj_matrix, h)
        return h / num_neighbours

    def _L1_gnn_ref(batch_graph, adj, W1, b1, W2, b2, W3, b3):
        import jax, jax.numpy as jnp
        import numpy as np
        B, N, F_IN, F_HID, F_OUT = (32, 512, 256, 256, 256)

        def _gcn_layer(x, adj, W, b):
            support = jnp.einsum('bnf,fh->bnh', x, W)
            return jnp.einsum('bnm,bmh->bnh', adj, support) + b
        x = jax.nn.relu(_gcn_layer(batch_graph, adj, W1, b1))
        x = jax.nn.relu(_gcn_layer(x, adj, W2, b2))
        out = _gcn_layer(x, adj, W3, b3)
        return out
    x = _layernorm(x + _L0_gnn_ref(x, adj, L0_gnn_W, L0_gnn_b), axis=-1)
    x = _layernorm(x + _L1_gnn_ref(x, adj, L1_gnn_W1, L1_gnn_b1, L1_gnn_W2, L1_gnn_b2, L1_gnn_W3, L1_gnn_b3), axis=-1)
    return x

_drawn_inputs = setup_inputs


def setup_inputs(seed=0):
    import zlib

    import numpy as np

    out = dict(_drawn_inputs(seed))
    spreads = {'L1_gnn_b1': (0.0, 0.1), 'L1_gnn_b2': (0.0, 0.1), 'L1_gnn_b3': (0.0, 0.1)}
    factors = {'L0_gnn_b': 4.781}
    for name, (base, spread) in spreads.items():
        noise = np.random.default_rng([zlib.crc32(name.encode()), seed]).standard_normal(out[name].shape)
        drawn = base * np.exp(spread * noise) if base else spread * noise
        out[name] = jnp.asarray(drawn.astype(out[name].dtype))
    for name, factor in factors.items():
        out[name] = (out[name] * factor).astype(out[name].dtype)
    return out
```

```python
from contextlib import ExitStack

import concourse.bass as bass
from concourse import mybir

ALU = mybir.AluOpType
ACT = mybir.ActivationFunctionType
F32 = mybir.dt.float32
F32R = mybir.dt.float32r

P = 128
RING = 3
DMA = 16
EPS = 1e-5
ONES = 2


def build(nc, xT, x, adjT, w0, w1, w2, w3, b0, b1, b2, b3, out):
    NB = x.shape[0]
    T = x.shape[2]
    F = x.shape[3]
    KF = F // P
    N = T * P
    TURNS = (NB - 1) // RING
    assert NB == TURNS * RING + 1

    with ExitStack() as ctx:
        def sb(name, shape, dt):
            return ctx.enter_context(nc.sbuf_tensor(name, shape, dt))

        def sem(name):
            return ctx.enter_context(nc.semaphore(name))

        xT_raw = sb("xT_raw", [P, KF, N], F32)
        x_raw = sb("x_raw", [P, T, F], F32)
        adj_raw = sb("adj_raw", [P, T, N], F32)
        w_raw = sb("w_raw", [P, 4, KF, F], F32)
        b0_all = sb("b0_all", [P, F], F32)
        b3_all = sb("b3_all", [P, F], F32)
        b1_col = sb("b1_col", [P, KF], F32)
        b2_col = sb("b2_col", [P, KF], F32)
        eps_col = sb("eps_col", [P, 1], F32)

        def pair(name, shape):
            return sb(name + "_hi", shape, F32R), sb(name + "_lo", shape, F32R)

        w_hi, w_lo = pair("w", [P, 4, KF, F])
        xT_hi, xT_lo = pair("xT", [P, KF, N])
        adj_hi, adj_lo = pair("adj", [P, RING, T, N])
        h_hi, h_lo = pair("h", [P, T, F + ONES])
        x1_hi, x1_lo = pair("x1", [P, T, F])
        g_hi, g_lo = pair("g", [P, KF, N])
        x2_hi, x2_lo = pair("x2", [P, KF, N])
        s2_hi, s2_lo = pair("s2", [P, T, F])
        x3_hi, x3_lo = pair("x3", [P, KF, N])
        s3_hi, s3_lo = pair("s3", [P, T, F])

        xb = sb("xb", [P, T, F], F32)
        v1 = sb("v1", [P, T, F], F32)
        x1 = sb("x1", [P, T, F], F32)
        x1b = sb("x1b", [P, RING, T, F], F32)
        relu = sb("relu", [P, KF, N], F32)
        v2 = sb("v2", [P, T, F], F32)
        y = sb("y", [P, T, F], F32)
        inv_rows = sb("inv_rows", [P, T], F32)
        stats1 = sb("stats1", [P, T, 6], F32)
        stats2 = sb("stats2", [P, T, 6], F32)
        moments1 = sb("moments1", [P, T, 2], F32)
        moments2 = sb("moments2", [P, T, 2], F32)
        std1 = sb("std1", [P, T], F32)
        std2 = sb("std2", [P, T], F32)
        rstd1 = sb("rstd1", [P, T], F32)
        rstd2 = sb("rstd2", [P, T], F32)

        bank_b = [ctx.enter_context(nc.psum_tensor(f"bank_b{j}", [P, 512], F32)) for j in range(T)]
        bank_a = [ctx.enter_context(nc.psum_tensor(f"bank_a{j}", [P, 512], F32)) for j in range(T)]

        w_loaded = [sem(f"w{n}_loaded") for n in range(4)]
        b_loaded = [sem(f"b{n}_loaded") for n in range(4)]
        xT_loaded = sem("xT_loaded")
        x_loaded = sem("x_loaded")
        adj_loaded = [sem(f"adj_half{n}_loaded") for n in range(2)]
        stored = sem("stored")
        eps_set = sem("eps_set")
        ones_set = sem("ones_set")
        w_hi_ready = sem("w_hi_ready")
        w_split = sem("w_split")
        xT_hi_ready = sem("xT_hi_ready")
        xT_split = sem("xT_split")
        adj_hi_ready = sem("adj_hi_ready")
        adj_split = sem("adj_split")
        xb_ready = sem("xb_ready")
        p0_done = sem("p0_done")
        p1_done = sem("p1_done")
        p2_done = sem("p2_done")
        p3_done = sem("p3_done")
        p4_done = sem("p4_done")
        p5_done = sem("p5_done")
        p6_done = sem("p6_done")
        p7_done = sem("p7_done")
        h_hi_ready = sem("h_hi_ready")
        h_split = sem("h_split")
        inv_ready = sem("inv_ready")
        v1_ready = sem("v1_ready")
        stats1_ready = sem("stats1_ready")
        moments1_ready = sem("moments1_ready")
        std1_ready = sem("std1_ready")
        rstd1_ready = sem("rstd1_ready")
        x1_ready = sem("x1_ready")
        x1b_ready = sem("x1b_ready")
        x1_hi_ready = sem("x1_hi_ready")
        x1_split = sem("x1_split")
        g_hi_ready = sem("g_hi_ready")
        g_split = sem("g_split")
        x2_hi_ready = sem("x2_hi_ready")
        x2_split = sem("x2_split")
        s2_hi_ready = sem("s2_hi_ready")
        s2_split = sem("s2_split")
        x3_hi_ready = sem("x3_hi_ready")
        x3_split = sem("x3_split")
        s3_hi_ready = sem("s3_hi_ready")
        s3_split = sem("s3_split")
        v2_ready = sem("v2_ready")
        stats2_ready = sem("stats2_ready")
        moments2_ready = sem("moments2_ready")
        std2_ready = sem("std2_ready")
        rstd2_ready = sem("rstd2_ready")
        y_ready = sem("y_ready")

        def at(batch, per, n):
            turn, r = batch
            return turn * (RING * per) + (r * per + n)

        def before(batch, n=1):
            return batch[0], batch[1] - n

        def slot(batch):
            return batch[1] % RING

        FIRST, LAST = (0, 0), (TURNS - 1, RING)

        def three_passes(pe, acc, st, mv, start, stop):
            pe.matmul(acc, st[0], mv[0], start=start, stop=False)
            pe.matmul(acc, st[0], mv[1], start=False, stop=False)
            return pe.matmul(acc, st[1], mv[0], start=False, stop=stop)

        block = ctx.enter_context(nc.Block())

        @block.sync
        def _(sp):
            sp.sem_inc(stored, DMA)
            sp.dma_start(w_raw[:, 0, :, :], w0).then_inc(w_loaded[0], DMA)
            sp.dma_start(xT_raw[:, :, :], xT[0]).then_inc(xT_loaded, DMA)
            for half in range(2):
                tiles = slice(half * T // 2, (half + 1) * T // 2)
                sp.dma_start(adj_raw[:, tiles, :], adjT[0, :, tiles, :]).then_inc(adj_loaded[half], DMA)
            sp.dma_start(x_raw[:, :, :], x[0]).then_inc(x_loaded, DMA)
            sp.dma_start(b0_all[:, :], b0.partition_broadcast(P)).then_inc(b_loaded[0], DMA)
            sp.dma_start(b1_col[:, :], b1).then_inc(b_loaded[1], DMA)
            sp.dma_start(b2_col[:, :], b2).then_inc(b_loaded[2], DMA)
            sp.dma_start(b3_all[:, :], b3.partition_broadcast(P)).then_inc(b_loaded[3], DMA)
            for n, w in ((1, w1), (2, w2), (3, w3)):
                sp.dma_start(w_raw[:, n, :, :], w).then_inc(w_loaded[n], DMA)

            def load(i):
                sp.wait_ge(xT_split, i * KF)
                sp.dma_start(xT_raw[:, :, :], xT[i]).then_inc(xT_loaded, DMA)
                sp.wait_ge(xb_ready, i * T)
                sp.dma_start(x_raw[:, :, :], x[i]).then_inc(x_loaded, DMA)
                for half in range(2):
                    tiles = slice(half * T // 2, (half + 1) * T // 2)
                    sp.wait_ge(adj_split, i * T + ((half + 1) * T // 2 - T))
                    sp.dma_start(adj_raw[:, tiles, :], adjT[i, :, tiles, :]).then_inc(adj_loaded[half], DMA)

            load(1)
            with sp.Fori(2, NB) as i:
                load(i)
                sp.wait_ge(y_ready, (i - 1) * T)
                sp.dma_start(out[i - 2], y[:, :, :]).then_inc(stored, DMA)
            sp.wait_ge(y_ready, (NB - 1) * T)
            sp.dma_start(out[NB - 2], y[:, :, :]).then_inc(stored, DMA)
            for j in range(T):
                sp.wait_ge(y_ready, (NB - 1) * T + j + 1)
                sp.dma_start(out[NB - 1, :, j, :], y[:, j, :]).then_inc(stored, DMA)
            sp.wait_ge(stored, (1 + NB - 1 + T) * DMA)

        @block.tensor
        def _(pe):
            def xw_product(done, bank, st, n, bank_free):
                for j in range(T):
                    cols = slice(j * P, (j + 1) * P)
                    bank_free(j)
                    for k in range(KF):
                        mm = three_passes(pe, bank[j][:, 0:F], (st[0][:, k, cols], st[1][:, k, cols]),
                                          (w_hi[:, n, k, :], w_lo[:, n, k, :]), k == 0, k == KF - 1)
                    mm.then_inc(done, 1)

            def p0(new, has_v2):
                pe.wait_ge(xT_split, at(new, KF, KF))

                def bank_free(j):
                    if has_v2:
                        pe.wait_ge(v2_ready, at(before(new), T, j + 1))

                xw_product(p0_done, bank_b, (xT_hi, xT_lo), 0, bank_free)

            def p1(new):
                pe.wait_ge(h_split, at(new, T, T))
                pe.wait_ge(adj_split, at(new, T, T))
                s = slot(new)
                for j in range(T):
                    cols = slice(j * P, (j + 1) * P)
                    for k in range(T):
                        mm = three_passes(pe, bank_b[j][:, 0:F + ONES],
                                          (adj_hi[:, s, k, cols], adj_lo[:, s, k, cols]),
                                          (h_hi[:, k, :], h_lo[:, k, :]), k == 0, k == T - 1)
                    mm.then_inc(p1_done, 1)

            def adj_product_T(batch, done, banks, st, split):
                s = slot(batch)
                for f in range(KF):
                    cols = slice(f * P, (f + 1) * P)
                    for k in range(T):
                        if f == 0:
                            pe.wait_ge(split, at(batch, T, k + 1))
                        mm = three_passes(pe, banks[f][:, :], (st[0][:, k, cols], st[1][:, k, cols]),
                                          (adj_hi[:, s, k, :], adj_lo[:, s, k, :]), k == 0, k == T - 1)
                    mm.then_inc(done, 1)

            def p2(new):
                adj_product_T(new, p2_done, bank_a[2:4], (x1_hi, x1_lo), x1_split)

            def p3(new):
                pe.wait_ge(g_split, at(new, KF, KF))
                for f in range(KF):
                    cols = slice(f * P, (f + 1) * P)
                    for k in range(KF):
                        mm = three_passes(pe, bank_a[f][:, :], (w_hi[:, 1, k, cols], w_lo[:, 1, k, cols]),
                                          (g_hi[:, k, :], g_lo[:, k, :]), k == 0, k == KF - 1)
                    mm.then_inc(p3_done, 1)

            def p4(old):
                pe.wait_ge(x2_split, at(old, KF, KF))
                xw_product(p4_done, bank_a, (x2_hi, x2_lo), 2, lambda j: None)

            def p5(old):
                pe.wait_ge(s2_split, at(old, T, T))
                adj_product_T(old, p5_done, bank_a[0:2], (s2_hi, s2_lo), s2_split)

            def p6(old, new):
                pe.wait_ge(x3_split, at(old, KF, KF))

                def bank_free(j):
                    if new is not None:
                        pe.wait_ge(v1_ready, at(new, T, j + 1))

                xw_product(p6_done, bank_b, (x3_hi, x3_lo), 3, bank_free)

            def p7(old):
                pe.wait_ge(s3_split, at(old, T, T))
                s = slot(old)
                for j in range(T):
                    cols = slice(j * P, (j + 1) * P)
                    for k in range(T):
                        mm = three_passes(pe, bank_b[j][:, 0:F],
                                          (adj_hi[:, s, k, cols], adj_lo[:, s, k, cols]),
                                          (s3_hi[:, k, :], s3_lo[:, k, :]), k == 0, k == T - 1)
                    mm.then_inc(p7_done, 1)

            def step(new):
                old = before(new)
                p0(new, True)
                p4(old)
                p1(new)
                p5(old)
                p2(new)
                p6(old, new)
                p3(new)
                p7(old)

            pe.wait_ge(w_split, 1)
            p0(FIRST, False)
            pe.wait_ge(ones_set, T)
            p1(FIRST)
            p2(FIRST)
            pe.wait_ge(w_split, 4)
            p3(FIRST)
            with pe.Fori(0, TURNS) as turn:
                for r in range(1, RING + 1):
                    step((turn, r))
            p4(LAST)
            p5(LAST)
            p6(LAST, None)
            p7(LAST)

        @block.scalar
        def _(act):
            def copy_hi(dst, src):
                return act.activation(dst, src, ACT.Copy)

            def split_w(n):
                act.wait_ge(w_loaded[n], DMA)
                copy_hi(w_hi[:, n, :, :], w_raw[:, n, :, :]).then_inc(w_hi_ready, 1)

            def split_xT(nxt, k):
                if k == 0:
                    act.wait_ge(xT_loaded, at(nxt, DMA, DMA))
                    if nxt is not FIRST:
                        act.wait_ge(p0_done, at(nxt, T, 0))
                copy_hi(xT_hi[:, k, :], xT_raw[:, k, :]).then_inc(xT_hi_ready, 1)

            def split_adj(nxt, k):
                if k % (T // 2) == 0:
                    act.wait_ge(adj_loaded[k // (T // 2)], at(nxt, DMA, DMA))
                copy_hi(adj_hi[:, slot(nxt), k, :], adj_raw[:, k, :]).then_inc(adj_hi_ready, 1)

            def h(new):
                for j in range(T):
                    act.wait_ge(p0_done, at(new, T, j + 1))
                    copy_hi(h_hi[:, j, 0:F], bank_b[j][:, 0:F]).then_inc(h_hi_ready, 1)

            def s2(old):
                for j in range(T):
                    act.wait_ge(p4_done, at(old, T, j + 1))
                    copy_hi(s2_hi[:, j, :], bank_a[j][:, 0:F]).then_inc(s2_hi_ready, 1)

            def s3(old):
                for j in range(T):
                    act.wait_ge(p6_done, at(old, T, j + 1))
                    copy_hi(s3_hi[:, j, :], bank_b[j][:, 0:F]).then_inc(s3_hi_ready, 1)

            def std_1(new, j):
                act.wait_ge(moments1_ready, at(new, T, j + 1))
                act.activation(std1[:, j:j + 1], moments1[:, j, 1:2], ACT.Sqrt,
                               bias=eps_col[:, :]).then_inc(std1_ready, 1)

            def x1_split_hi(new, j):
                act.wait_ge(x1_ready, at(new, T, j + 1))
                copy_hi(x1_hi[:, j, :], x1[:, j, :]).then_inc(x1_hi_ready, 1)

            def norm1(new):
                for j in range(T + 1):
                    if j < T:
                        std_1(new, j)
                    if j >= 1:
                        x1_split_hi(new, j - 1)

            def g(new, f):
                act.wait_ge(p2_done, at(new, KF, f + 1))
                copy_hi(g_hi[:, f, :], bank_a[2 + f][:, :]).then_inc(g_hi_ready, 1)

            def relu_split(done, batch, f, bias, hi, ready):
                act.wait_ge(done, at(batch, KF, f + 1))
                act.activation(relu[:, f, :], bank_a[f][:, :], ACT.Relu, bias=bias[:, f:f + 1])
                act.activation(hi[:, f, :], bank_a[f][:, :], ACT.Relu,
                               bias=bias[:, f:f + 1]).then_inc(ready, 1)

            def x2(new, f):
                if f == 0 and new is not FIRST:
                    act.wait_ge(x3_split, at(before(new), KF, KF))
                relu_split(p3_done, new, f, b1_col, x2_hi, x2_hi_ready)

            def x3(old, f):
                if f == 0:
                    act.wait_ge(x2_split, at(old, KF, KF))
                relu_split(p5_done, old, f, b2_col, x3_hi, x3_hi_ready)

            def norm2(old):
                for j in range(T):
                    act.wait_ge(moments2_ready, at(old, T, j + 1))
                    act.activation(std2[:, j:j + 1], moments2[:, j, 1:2], ACT.Sqrt,
                                   bias=eps_col[:, :]).then_inc(std2_ready, 1)

            def step(new, last=False):
                old, nxt = before(new), before(new, -1)
                h(new)
                s2(old)
                norm1(new)
                if not last:
                    split_adj(nxt, 0)
                x3(old, 0)
                if not last:
                    split_adj(nxt, 1)
                    split_adj(nxt, 2)
                x3(old, 1)
                if not last:
                    split_adj(nxt, 3)
                g(new, 0)
                if not last:
                    for k in range(KF):
                        split_xT(nxt, k)
                g(new, 1)
                s3(old)
                x2(new, 0)
                x2(new, 1)
                norm2(old)

            split_w(0)
            for k in range(KF):
                split_xT(FIRST, k)
            for k in range(T):
                split_adj(FIRST, k)
            h(FIRST)
            act.wait_ge(eps_set, 1)
            norm1(FIRST)
            for n in range(1, 4):
                split_w(n)
            g(FIRST, 0)
            g(FIRST, 1)
            act.wait_ge(b_loaded[1], DMA)
            act.wait_ge(b_loaded[2], DMA)
            x2(FIRST, 0)
            x2(FIRST, 1)
            for k in range(KF):
                split_xT(before(FIRST, -1), k)
            for k in range(T):
                split_adj(before(FIRST, -1), k)
            with act.Fori(0, TURNS - 1) as turn:
                for r in range(1, RING + 1):
                    step((turn, r))
            for r in range(1, RING + 1):
                step((TURNS - 1, r), last=r == RING)
            s2(LAST)
            x3(LAST, 0)
            x3(LAST, 1)
            s3(LAST)
            norm2(LAST)

        @block.vector
        def _(dve):
            def sub_hi(lo, full, hi):
                return dve.tensor_tensor(lo, full, hi.bitcast(F32), ALU.subtract)

            def split_w(n):
                dve.wait_ge(w_hi_ready, n + 1)
                sub_hi(w_lo[:, n, :, :], w_raw[:, n, :, :], w_hi[:, n, :, :]).then_inc(w_split, 1)

            def split_xT(nxt, k):
                dve.wait_ge(xT_hi_ready, at(nxt, KF, k + 1))
                sub_hi(xT_lo[:, k, :], xT_raw[:, k, :], xT_hi[:, k, :]).then_inc(xT_split, 1)

            def split_adj(nxt, k):
                s = slot(nxt)
                dve.wait_ge(adj_hi_ready, at(nxt, T, k + 1))
                sub_hi(adj_lo[:, s, k, :], adj_raw[:, k, :], adj_hi[:, s, k, :]).then_inc(adj_split, 1)

            def h(new):
                for j in range(T):
                    dve.wait_ge(h_hi_ready, at(new, T, j + 1))
                    sub_hi(h_lo[:, j, 0:F], bank_b[j][:, 0:F], h_hi[:, j, 0:F]).then_inc(h_split, 1)

            def s2(old):
                for j in range(T):
                    dve.wait_ge(s2_hi_ready, at(old, T, j + 1))
                    sub_hi(s2_lo[:, j, :], bank_a[j][:, 0:F], s2_hi[:, j, :]).then_inc(s2_split, 1)

            def s3(old):
                for j in range(T):
                    dve.wait_ge(s3_hi_ready, at(old, T, j + 1))
                    sub_hi(s3_lo[:, j, :], bank_b[j][:, 0:F], s3_hi[:, j, :]).then_inc(s3_split, 1)

            def norm1(new):
                dve.wait_ge(xb_ready, at(new, T, T))
                if new is not FIRST:
                    dve.wait_ge(x1b_ready, at(new, T, 0))
                for j in range(T + 2):
                    a, b, c = j, j - 1, j - 2
                    if a < T:
                        dve.wait_ge(p1_done, at(new, T, a + 1))
                        dve.reciprocal(inv_rows[:, a:a + 1], bank_b[a][:, F:F + 1]).then_inc(inv_ready, 1)
                    if 0 <= b < T:
                        dve.wait_ge(std1_ready, at(new, T, b + 1))
                        dve.reciprocal(rstd1[:, b:b + 1], std1[:, b:b + 1]).then_inc(rstd1_ready, 1)
                    if a < T:
                        dve.wait_ge(inv_ready, at(new, T, a + 1))
                        dve.scalar_tensor_tensor(v1[:, a, :], bank_b[a][:, 0:F], inv_rows[:, a:a + 1], xb[:, a, :],
                                                 ALU.mult, ALU.add).then_inc(v1_ready, 1)
                    if 0 <= b < T:
                        dve.wait_ge(rstd1_ready, at(new, T, b + 1))
                        dve.tensor_scalar(x1[:, b, :], v1[:, b, :], moments1[:, b, 0:1], rstd1[:, b:b + 1],
                                          ALU.subtract, ALU.mult).then_inc(x1_ready, 1)
                    if a < T:
                        dve.wait_ge(v1_ready, at(new, T, a + 1))
                        dve.bn_stats(stats1[:, a, :], v1[:, a, :]).then_inc(stats1_ready, 1)
                    if 0 <= c < T:
                        dve.wait_ge(x1_hi_ready, at(new, T, c + 1))
                        sub_hi(x1_lo[:, c, :], x1[:, c, :], x1_hi[:, c, :]).then_inc(x1_split, 1)
                    if a < T:
                        dve.wait_ge(eps_set, 1)
                        dve.wait_ge(stats1_ready, at(new, T, a + 1))
                        dve.bn_aggr(moments1[:, a, :], stats1[:, a, :]).then_inc(moments1_ready, 1)

            def g(new, f):
                dve.wait_ge(g_hi_ready, at(new, KF, f + 1))
                sub_hi(g_lo[:, f, :], bank_a[2 + f][:, :], g_hi[:, f, :]).then_inc(g_split, 1)

            def x2(new, f):
                dve.wait_ge(x2_hi_ready, at(new, KF, f + 1))
                sub_hi(x2_lo[:, f, :], relu[:, f, :], x2_hi[:, f, :]).then_inc(x2_split, 1)

            def x3(old, f):
                dve.wait_ge(x3_hi_ready, at(old, KF, f + 1))
                sub_hi(x3_lo[:, f, :], relu[:, f, :], x3_hi[:, f, :]).then_inc(x3_split, 1)

            def norm2(old):
                dve.wait_ge(x1b_ready, at(old, T, T))
                dve.wait_ge(stored, at(old, DMA, DMA))
                for j in range(T + 1):
                    a, b = j, j - 1
                    if a < T:
                        dve.wait_ge(p7_done, at(old, T, a + 1))
                        dve.tensor_tensor(v2[:, a, :], bank_b[a][:, 0:F], x1b[:, slot(old), a, :],
                                          ALU.add).then_inc(v2_ready, 1)
                    if b >= 0:
                        dve.wait_ge(std2_ready, at(old, T, b + 1))
                        dve.reciprocal(rstd2[:, b:b + 1], std2[:, b:b + 1]).then_inc(rstd2_ready, 1)
                    if a < T:
                        dve.wait_ge(v2_ready, at(old, T, T + a + 1))
                        dve.bn_stats(stats2[:, a, :], v2[:, a, :]).then_inc(stats2_ready, 1)
                    if b >= 0:
                        dve.wait_ge(rstd2_ready, at(old, T, b + 1))
                        dve.tensor_scalar(y[:, b, :], v2[:, b, :], moments2[:, b, 0:1], rstd2[:, b:b + 1],
                                          ALU.subtract, ALU.mult).then_inc(y_ready, 1)
                    if a < T:
                        dve.wait_ge(eps_set, 1)
                        dve.wait_ge(stats2_ready, at(old, T, a + 1))
                        dve.bn_aggr(moments2[:, a, :], stats2[:, a, :]).then_inc(moments2_ready, 1)

            def step(new, last=False):
                old, nxt = before(new), before(new, -1)
                h(new)
                s2(old)
                norm1(new)
                if not last:
                    split_adj(nxt, 0)
                x3(old, 0)
                if not last:
                    split_adj(nxt, 1)
                    split_adj(nxt, 2)
                x3(old, 1)
                if not last:
                    split_adj(nxt, 3)
                g(new, 0)
                if not last:
                    for k in range(KF):
                        split_xT(nxt, k)
                g(new, 1)
                s3(old)
                x2(new, 0)
                x2(new, 1)
                norm2(old)

            dve.memset(eps_col[:, :], EPS).then_inc(eps_set, 1)
            for j in range(T):
                dve.memset(h_hi[:, j, F:F + ONES].bitcast(F32), 1.0).then_inc(ones_set, 1)
                dve.memset(h_lo[:, j, F:F + ONES].bitcast(F32), 0.0).then_inc(v2_ready, 1)
            split_w(0)
            for k in range(KF):
                split_xT(FIRST, k)
            for k in range(T):
                split_adj(FIRST, k)
            h(FIRST)
            norm1(FIRST)
            for n in range(1, 4):
                split_w(n)
            g(FIRST, 0)
            g(FIRST, 1)
            x2(FIRST, 0)
            x2(FIRST, 1)
            for k in range(KF):
                split_xT(before(FIRST, -1), k)
            for k in range(T):
                split_adj(before(FIRST, -1), k)
            with dve.Fori(0, TURNS - 1) as turn:
                for r in range(1, RING + 1):
                    step((turn, r))
            for r in range(1, RING + 1):
                step((TURNS - 1, r), last=r == RING)
            s2(LAST)
            x3(LAST, 0)
            x3(LAST, 1)
            s3(LAST)
            norm2(LAST)

        @block.gpsimd
        def _(pool):
            def add_b0(batch):
                pool.wait_ge(x_loaded, at(batch, DMA, DMA))
                for j in range(T):
                    if batch is not FIRST:
                        pool.wait_ge(v1_ready, at(batch, T, j + 1 - T))
                    pool.tensor_tensor(xb[:, j, :], x_raw[:, j, :], b0_all[:, :], ALU.add).then_inc(xb_ready, 1)

            def add_b3(batch):
                for j in range(T):
                    pool.wait_ge(x1_ready, at(batch, T, j + 1))
                    pool.tensor_tensor(x1b[:, slot(batch), j, :], x1[:, j, :], b3_all[:, :],
                                       ALU.add).then_inc(x1b_ready, 1)

            pool.wait_ge(b_loaded[0], DMA)
            add_b0(FIRST)
            pool.wait_ge(b_loaded[3], DMA)
            add_b3(FIRST)
            with pool.Fori(0, TURNS) as turn:
                for r in range(1, RING + 1):
                    add_b0((turn, r))
                    add_b3((turn, r))


def kernel(**inputs):
    import numpy as np
    import concourse.bacc as bacc
    from concourse.bass_utils import run_bass_kernel_spmd

    x = np.asarray(inputs["x"])
    adj = np.asarray(inputs["adj"])
    NB, N, F = x.shape
    T, KF = N // P, F // P
    arrays = {
        "xT": x.reshape(NB, P, T, KF, P).transpose(0, 4, 3, 2, 1).reshape(NB, P, KF, N),
        "x": x.reshape(NB, P, T, F),
        "adjT": adj.reshape(NB, P, T, P, T).transpose(0, 3, 4, 2, 1).reshape(NB, P, T, N),
    }
    for n, name in enumerate(("L0_gnn_W", "L1_gnn_W1", "L1_gnn_W2", "L1_gnn_W3")):
        arrays[f"w{n}"] = np.asarray(inputs[name]).reshape(KF, P, F).transpose(1, 0, 2)
    arrays["b0"] = np.asarray(inputs["L0_gnn_b"])
    arrays["b1"] = np.asarray(inputs["L1_gnn_b1"]).reshape(KF, P).T
    arrays["b2"] = np.asarray(inputs["L1_gnn_b2"]).reshape(KF, P).T
    arrays["b3"] = np.asarray(inputs["L1_gnn_b3"])
    arrays = {f"in_{k}": np.ascontiguousarray(a) for k, a in arrays.items()}

    nc = bacc.Bacc("TRN2", target_bir_lowering=False, num_devices=1)
    args = [nc.dram_tensor(k, a.shape, mybir.dt.from_np(a.dtype), kind="ExternalInput").ap()
            for k, a in arrays.items()]
    y = nc.dram_tensor("out_y", (NB, P, T, F), F32, kind="ExternalOutput").ap()
    build(nc, *args, y)
    r = run_bass_kernel_spmd(nc, [arrays], core_ids=[0])
    return r.results[0]["out_y"].reshape(NB, N, F)
```

```python
from contextlib import ExitStack

import concourse.bass as bass
from concourse import mybir

ALU = mybir.AluOpType
ACT = mybir.ActivationFunctionType
F32 = mybir.dt.float32
F32R = mybir.dt.float32r

P = 128
RING = 3
DMA = 16
EPS = 1e-5
ONES = 2


def build(nc, xT, x, adjT, w0, w1, w2, w3, b0, b1, b2, b3, out):
    NB = x.shape[0]
    T = x.shape[2]
    F = x.shape[3]
    KF = F // P
    N = T * P
    TURNS = (NB - 1) // RING
    assert NB == TURNS * RING + 1

    with ExitStack() as ctx:
        def sb(name, shape, dt):
            return ctx.enter_context(nc.sbuf_tensor(name, shape, dt))

        def sem(name):
            return ctx.enter_context(nc.semaphore(name))

        xT_raw = sb("xT_raw", [P, KF, N], F32)
        x_raw = sb("x_raw", [P, T, F], F32)
        adj_raw = sb("adj_raw", [P, T, N], F32)
        w_raw = sb("w_raw", [P, 4, KF, F], F32)
        b0_all = sb("b0_all", [P, F], F32)
        b3_all = sb("b3_all", [P, F], F32)
        b1_col = sb("b1_col", [P, KF], F32)
        b2_col = sb("b2_col", [P, KF], F32)
        eps_col = sb("eps_col", [P, 1], F32)
        sqrt_eps = sb("sqrt_eps", [P, 1], F32)

        def pair(name, shape):
            return sb(name + "_hi", shape, F32R), sb(name + "_lo", shape, F32R)

        w_hi, w_lo = pair("w", [P, 4, KF, F])
        xT_hi, xT_lo = pair("xT", [P, KF, N])
        adj_hi, adj_lo = pair("adj", [P, RING, T, N])
        h_hi, h_lo = pair("h", [P, T, F + ONES])
        x1_hi, x1_lo = pair("x1", [P, T, F])
        g_hi, g_lo = pair("g", [P, KF, N])
        x2_hi, x2_lo = pair("x2", [P, KF, N])
        s2_hi, s2_lo = pair("s2", [P, T, F])
        x3_hi, x3_lo = pair("x3", [P, KF, N])
        s3_hi, s3_lo = pair("s3", [P, T, F])

        xb = sb("xb", [P, T, F], F32)
        v1 = sb("v1", [P, T, F], F32)
        x1 = sb("x1", [P, T, F], F32)
        x1b = sb("x1b", [P, RING, T, F], F32)
        relu = sb("relu", [P, KF, N], F32)
        v2 = sb("v2", [P, T, F], F32)
        y = sb("y", [P, T, F], F32)
        inv_rows = sb("inv_rows", [P, T], F32)
        stats1 = sb("stats1", [P, T, 6], F32)
        stats2 = sb("stats2", [P, T, 6], F32)
        moments1 = sb("moments1", [P, T, 2], F32)
        moments2 = sb("moments2", [P, T, 2], F32)
        std1 = sb("std1", [P, T], F32)
        std2 = sb("std2", [P, T], F32)
        rstd1 = sb("rstd1", [P, T], F32)
        rstd2 = sb("rstd2", [P, T], F32)

        bank_b = [ctx.enter_context(nc.psum_tensor(f"bank_b{j}", [P, 512], F32)) for j in range(T)]
        bank_a = [ctx.enter_context(nc.psum_tensor(f"bank_a{j}", [P, 512], F32)) for j in range(T)]

        w_loaded = [sem(f"w{n}_loaded") for n in range(4)]
        b_loaded = [sem(f"b{n}_loaded") for n in range(4)]
        xT_loaded = [sem(f"xT_half{n}_loaded") for n in range(2)]
        x_loaded = sem("x_loaded")
        adj_loaded = [sem(f"adj_half{n}_loaded") for n in range(2)]
        stored = sem("stored")
        eps_set = sem("eps_set")
        ones_set = sem("ones_set")
        w_hi_ready = sem("w_hi_ready")
        w_split = sem("w_split")
        w0_hi_ready = sem("w0_hi_ready")
        w0_split = sem("w0_split")
        xT_hi_ready = sem("xT_hi_ready")
        xT_split = sem("xT_split")
        adj_hi_ready = sem("adj_hi_ready")
        adj_split = sem("adj_split")
        xb_ready = sem("xb_ready")
        p0_done = sem("p0_done")
        p1_done = sem("p1_done")
        p2_done = sem("p2_done")
        p3_done = sem("p3_done")
        p4_done = sem("p4_done")
        p5_done = sem("p5_done")
        p6_done = sem("p6_done")
        p7_done = sem("p7_done")
        h_hi_ready = sem("h_hi_ready")
        h_split = sem("h_split")
        inv_ready = sem("inv_ready")
        v1_ready = sem("v1_ready")
        stats1_ready = sem("stats1_ready")
        moments1_ready = sem("moments1_ready")
        std1_ready = sem("std1_ready")
        rstd1_ready = sem("rstd1_ready")
        x1_ready = sem("x1_ready")
        x1b_ready = sem("x1b_ready")
        x1_hi_ready = sem("x1_hi_ready")
        x1_split = sem("x1_split")
        g_hi_ready = sem("g_hi_ready")
        g_split = sem("g_split")
        x2_hi_ready = sem("x2_hi_ready")
        x2_split = sem("x2_split")
        s2_hi_ready = sem("s2_hi_ready")
        s2_split = sem("s2_split")
        x3_hi_ready = sem("x3_hi_ready")
        x3_split = sem("x3_split")
        s3_hi_ready = sem("s3_hi_ready")
        s3_split = sem("s3_split")
        v2_ready = sem("v2_ready")
        stats2_ready = sem("stats2_ready")
        moments2_ready = sem("moments2_ready")
        std2_ready = sem("std2_ready")
        rstd2_ready = sem("rstd2_ready")
        y_ready = sem("y_ready")

        def at(batch, per, n):
            turn, r = batch
            return turn * (RING * per) + (r * per + n)

        def before(batch, n=1):
            return batch[0], batch[1] - n

        def slot(batch):
            return batch[1] % RING

        FIRST, LAST = (0, 0), (TURNS - 1, RING)

        def three_passes(pe, acc, st, mv, start, stop):
            pe.matmul(acc, st[0], mv[0], start=start, stop=False)
            pe.matmul(acc, st[0], mv[1], start=False, stop=False)
            return pe.matmul(acc, st[1], mv[0], start=False, stop=stop)

        block = ctx.enter_context(nc.Block())

        @block.sync
        def _(sp):
            sp.sem_inc(stored, DMA)
            def half_of(half, n):
                return slice(half * n // 2, (half + 1) * n // 2)

            for half in range(2):
                cols = half_of(half, N)
                sp.dma_start(xT_raw[:, :, cols], xT[0, :, :, cols]).then_inc(xT_loaded[half], DMA)
            for half in range(2):
                tiles = half_of(half, T)
                sp.dma_start(adj_raw[:, tiles, :], adjT[0, :, tiles, :]).then_inc(adj_loaded[half], DMA)
            sp.dma_start(x_raw[:, :, :], x[0]).then_inc(x_loaded, DMA)
            sp.dma_start(b0_all[:, :], b0.partition_broadcast(P)).then_inc(b_loaded[0], DMA)
            sp.dma_start(b1_col[:, :], b1).then_inc(b_loaded[1], DMA)
            sp.dma_start(b2_col[:, :], b2).then_inc(b_loaded[2], DMA)

            def load(i):
                for half in range(2):
                    cols = half_of(half, N)
                    sp.wait_ge(xT_split, i * 2 + (half - 1))
                    sp.dma_start(xT_raw[:, :, cols], xT[i, :, :, cols]).then_inc(xT_loaded[half], DMA)
                sp.wait_ge(xb_ready, i * T)
                sp.dma_start(x_raw[:, :, :], x[i]).then_inc(x_loaded, DMA)
                for half in range(2):
                    tiles = half_of(half, T)
                    sp.wait_ge(adj_split, i * T + ((half + 1) * T // 2 - T))
                    sp.dma_start(adj_raw[:, tiles, :], adjT[i, :, tiles, :]).then_inc(adj_loaded[half], DMA)

            load(1)
            sp.dma_start(b3_all[:, :], b3.partition_broadcast(P)).then_inc(b_loaded[3], DMA)
            for n, w in ((1, w1), (2, w2), (3, w3)):
                sp.dma_start(w_raw[:, n, :, :], w).then_inc(w_loaded[n], DMA)
            with sp.Fori(2, NB) as i:
                load(i)
                sp.wait_ge(y_ready, (i - 1) * T)
                sp.dma_start(out[i - 2], y[:, :, :]).then_inc(stored, DMA)
            sp.wait_ge(y_ready, (NB - 1) * T)
            sp.dma_start(out[NB - 2], y[:, :, :]).then_inc(stored, DMA)
            for j in range(T):
                sp.wait_ge(y_ready, (NB - 1) * T + j + 1)
                sp.dma_start(out[NB - 1, :, j, :], y[:, j, :]).then_inc(stored, DMA)
            sp.wait_ge(stored, (1 + NB - 1 + T) * DMA)

        @block.tensor
        def _(pe):
            def xw_product(done, bank, st, n, ready):
                for j in range(T):
                    cols = slice(j * P, (j + 1) * P)
                    ready(j)
                    for k in range(KF):
                        mm = three_passes(pe, bank[j][:, 0:F], (st[0][:, k, cols], st[1][:, k, cols]),
                                          (w_hi[:, n, k, :], w_lo[:, n, k, :]), k == 0, k == KF - 1)
                    mm.then_inc(done, 1)

            def p0(nxt, reader, read):
                def ready(j):
                    if j % (T // 2) == 0:
                        pe.wait_ge(xT_split, at(nxt, 2, j // (T // 2) + 1))
                    if reader is not None:
                        pe.wait_ge(reader, at(read, T, j + 1))

                xw_product(p0_done, bank_b, (xT_hi, xT_lo), 0, ready)

            def p1(new, tiles=range(T)):
                pe.wait_ge(h_split, at(new, T, T))
                pe.wait_ge(adj_split, at(new, T, T))
                s = slot(new)
                for j in tiles:
                    cols = slice(j * P, (j + 1) * P)
                    for k in range(T):
                        mm = three_passes(pe, bank_b[j][:, 0:F + ONES],
                                          (adj_hi[:, s, k, cols], adj_lo[:, s, k, cols]),
                                          (h_hi[:, k, :], h_lo[:, k, :]), k == 0, k == T - 1)
                    mm.then_inc(p1_done, 1)

            def adj_product_T(batch, done, banks, st, split):
                s = slot(batch)
                for f in range(KF):
                    cols = slice(f * P, (f + 1) * P)
                    for k in range(T):
                        if f == 0:
                            pe.wait_ge(split, at(batch, T, k + 1))
                        mm = three_passes(pe, banks[f][:, :], (st[0][:, k, cols], st[1][:, k, cols]),
                                          (adj_hi[:, s, k, :], adj_lo[:, s, k, :]), k == 0, k == T - 1)
                    mm.then_inc(done, 1)

            def p2(new):
                adj_product_T(new, p2_done, bank_a[2:4], (x1_hi, x1_lo), x1_split)

            def p3(new):
                pe.wait_ge(g_split, at(new, KF, KF))
                for f in range(KF):
                    cols = slice(f * P, (f + 1) * P)
                    for k in range(KF):
                        mm = three_passes(pe, bank_a[f][:, :], (w_hi[:, 1, k, cols], w_lo[:, 1, k, cols]),
                                          (g_hi[:, k, :], g_lo[:, k, :]), k == 0, k == KF - 1)
                    mm.then_inc(p3_done, 1)

            def p4(old):
                pe.wait_ge(x2_split, at(old, KF, KF))
                xw_product(p4_done, bank_a, (x2_hi, x2_lo), 2, lambda j: None)

            def p5(old):
                pe.wait_ge(s2_split, at(old, T, T))
                adj_product_T(old, p5_done, bank_a[0:2], (s2_hi, s2_lo), s2_split)

            def p6(old, reader, read):
                pe.wait_ge(x3_split, at(old, KF, KF))
                xw_product(p6_done, bank_b, (x3_hi, x3_lo), 3,
                           lambda j: pe.wait_ge(reader, at(read, T, j + 1)))

            def p7(old, tiles=range(T)):
                pe.wait_ge(s3_split, at(old, T, T))
                s = slot(old)
                for j in tiles:
                    cols = slice(j * P, (j + 1) * P)
                    for k in range(T):
                        mm = three_passes(pe, bank_b[j][:, 0:F],
                                          (adj_hi[:, s, k, cols], adj_lo[:, s, k, cols]),
                                          (s3_hi[:, k, :], s3_lo[:, k, :]), k == 0, k == T - 1)
                    mm.then_inc(p7_done, 1)

            def step(new):
                old, nxt = before(new), before(new, -1)
                p5(old)
                p2(new)
                p6(old, v1_ready, new)
                p3(new)
                p7(old)
                p0(nxt, v2_ready, old)
                p4(new)
                p1(nxt)

            pe.wait_ge(w0_split, 1)
            p0(FIRST, None, None)
            pe.wait_ge(ones_set, 2 * T)
            p1(FIRST)
            second = before(FIRST, -1)
            p0(second, v1_ready, FIRST)
            p2(FIRST)
            p1(second, range(0, 1))
            pe.wait_ge(w_split, 1)
            p3(FIRST)
            p1(second, range(1, 3))
            pe.wait_ge(w_split, 3)
            p4(FIRST)
            p1(second, range(3, T))
            with pe.Fori(0, TURNS - 1) as turn:
                for r in range(1, RING + 1):
                    step((turn, r))
            for r in range(1, RING):
                step((TURNS - 1, r))
            old = before(LAST)
            p5(old)
            p2(LAST)
            p6(old, v1_ready, LAST)
            p3(LAST)
            p7(old, range(0, 2))
            p4(LAST)
            p7(old, range(2, 3))
            p5(LAST)
            p7(old, range(3, T))
            p6(LAST, v2_ready, old)
            p7(LAST)

        @block.scalar
        def _(act):
            def copy_hi(dst, src):
                return act.activation(dst, src, ACT.Copy)

            def split_w(n):
                act.wait_ge(w_loaded[n], DMA)
                copy_hi(w_hi[:, n, :, :], w_raw[:, n, :, :]).then_inc(w_hi_ready, 1)

            def split_xT(nxt, half):
                cols = slice(half * N // 2, (half + 1) * N // 2)
                act.wait_ge(xT_loaded[half], at(nxt, DMA, DMA))
                if nxt is not FIRST:
                    act.wait_ge(p0_done, at(nxt, T, 0))
                copy_hi(xT_hi[:, :, cols], xT_raw[:, :, cols]).then_inc(xT_hi_ready, 1)

            def split_adj(nxt, k):
                if k % (T // 2) == 0:
                    act.wait_ge(adj_loaded[k // (T // 2)], at(nxt, DMA, DMA))
                copy_hi(adj_hi[:, slot(nxt), k, :], adj_raw[:, k, :]).then_inc(adj_hi_ready, 1)

            def h(new):
                for j in range(T):
                    act.wait_ge(p0_done, at(new, T, j + 1))
                    copy_hi(h_hi[:, j, 0:F], bank_b[j][:, 0:F]).then_inc(h_hi_ready, 1)

            def s2(old):
                for j in range(T):
                    act.wait_ge(p4_done, at(old, T, j + 1))
                    copy_hi(s2_hi[:, j, :], bank_a[j][:, 0:F]).then_inc(s2_hi_ready, 1)

            def s3(old):
                for j in range(T):
                    act.wait_ge(p6_done, at(old, T, j + 1))
                    copy_hi(s3_hi[:, j, :], bank_b[j][:, 0:F]).then_inc(s3_hi_ready, 1)

            def std_1(new, j):
                act.wait_ge(moments1_ready, at(new, T, j + 1))
                act.activation(std1[:, j:j + 1], moments1[:, j, 1:2], ACT.Sqrt,
                               bias=eps_col[:, :]).then_inc(std1_ready, 1)

            def x1_split_hi(new, j):
                act.wait_ge(x1_ready, at(new, T, j + 1))
                copy_hi(x1_hi[:, j, :], x1[:, j, :]).then_inc(x1_hi_ready, 1)

            def norm1(new, turns=range(T + 1)):
                for j in turns:
                    if j < T:
                        std_1(new, j)
                    if j >= 1:
                        x1_split_hi(new, j - 1)

            def g(new, f):
                act.wait_ge(p2_done, at(new, KF, f + 1))
                copy_hi(g_hi[:, f, :], bank_a[2 + f][:, :]).then_inc(g_hi_ready, 1)

            def relu_split(done, batch, f, bias, hi, ready):
                act.wait_ge(done, at(batch, KF, f + 1))
                act.activation(relu[:, f, :], bank_a[f][:, :], ACT.Relu, bias=bias[:, f:f + 1])
                act.activation(hi[:, f, :], bank_a[f][:, :], ACT.Relu,
                               bias=bias[:, f:f + 1]).then_inc(ready, 1)

            def x2(new, f):
                if f == 0 and new is not FIRST:
                    act.wait_ge(x3_split, at(before(new), KF, KF))
                relu_split(p3_done, new, f, b1_col, x2_hi, x2_hi_ready)

            def x3(old, f):
                if f == 0:
                    act.wait_ge(x2_split, at(old, KF, KF))
                relu_split(p5_done, old, f, b2_col, x3_hi, x3_hi_ready)

            def norm2(old, tiles=range(T)):
                for j in tiles:
                    act.wait_ge(moments2_ready, at(old, T, j + 1))
                    act.activation(std2[:, j:j + 1], moments2[:, j, 1:2], ACT.Sqrt,
                                   bias=eps_col[:, :]).then_inc(std2_ready, 1)

            def step(new, last=False):
                old, nxt = before(new), before(new, -1)
                if not last:
                    split_adj(nxt, 0)
                x3(old, 0)
                if not last:
                    split_adj(nxt, 1)
                    split_adj(nxt, 2)
                x3(old, 1)
                if not last:
                    split_adj(nxt, 3)
                g(new, 0)
                if not last:
                    split_xT(nxt, 0)
                    split_xT(nxt, 1)
                g(new, 1)
                s3(old)
                x2(new, 0)
                x2(new, 1)
                if not last:
                    norm2(old)
                    h(nxt)
                    s2(new)
                    norm1(nxt)

            act.dma_start(w_raw[:, 0, :, :], w0).then_inc(w_loaded[0], DMA)
            act.wait_ge(eps_set, 1)
            act.activation(sqrt_eps[:, :], eps_col[:, :], ACT.Sqrt)
            second = before(FIRST, -1)
            split_xT(FIRST, 0)
            split_xT(FIRST, 1)
            for k in range(T):
                split_adj(FIRST, k)
            h(FIRST)
            split_xT(second, 0)
            split_xT(second, 1)
            norm1(FIRST)
            split_w(1)
            h(second)
            for k in range(T):
                split_adj(second, k)
            g(FIRST, 0)
            g(FIRST, 1)
            split_w(2)
            norm1(second, range(0, 1))
            split_w(3)
            act.wait_ge(b_loaded[1], DMA)
            act.wait_ge(b_loaded[2], DMA)
            x2(FIRST, 0)
            x2(FIRST, 1)
            norm1(second, range(1, 2))
            s2(FIRST)
            norm1(second, range(2, T + 1))
            with act.Fori(0, TURNS - 1) as turn:
                for r in range(1, RING + 1):
                    step((turn, r))
            for r in range(1, RING + 1):
                step((TURNS - 1, r), last=r == RING)
            norm2(before(LAST), range(0, 2))
            s2(LAST)
            norm2(before(LAST), range(2, 3))
            x3(LAST, 0)
            x3(LAST, 1)
            norm2(before(LAST), range(3, T))
            s3(LAST)
            norm2(LAST)

        @block.vector
        def _(dve):
            def sub_hi(lo, full, hi):
                return dve.tensor_tensor(lo, full, hi.bitcast(F32), ALU.subtract)

            def split_w(n):
                dve.wait_ge(w_hi_ready, n)
                sub_hi(w_lo[:, n, :, :], w_raw[:, n, :, :], w_hi[:, n, :, :]).then_inc(w_split, 1)

            def split_xT(nxt, half):
                cols = slice(half * N // 2, (half + 1) * N // 2)
                dve.wait_ge(xT_hi_ready, at(nxt, 2, half + 1))
                sub_hi(xT_lo[:, :, cols], xT_raw[:, :, cols], xT_hi[:, :, cols]).then_inc(xT_split, 1)

            def split_adj(nxt, k):
                s = slot(nxt)
                dve.wait_ge(adj_hi_ready, at(nxt, T, k + 1))
                sub_hi(adj_lo[:, s, k, :], adj_raw[:, k, :], adj_hi[:, s, k, :]).then_inc(adj_split, 1)

            def h(new):
                for j in range(T):
                    dve.wait_ge(h_hi_ready, at(new, T, j + 1))
                    sub_hi(h_lo[:, j, 0:F], bank_b[j][:, 0:F], h_hi[:, j, 0:F]).then_inc(h_split, 1)

            def s2(old):
                for j in range(T):
                    dve.wait_ge(s2_hi_ready, at(old, T, j + 1))
                    sub_hi(s2_lo[:, j, :], bank_a[j][:, 0:F], s2_hi[:, j, :]).then_inc(s2_split, 1)

            def s3(old):
                for j in range(T):
                    dve.wait_ge(s3_hi_ready, at(old, T, j + 1))
                    sub_hi(s3_lo[:, j, :], bank_b[j][:, 0:F], s3_hi[:, j, :]).then_inc(s3_split, 1)

            def norm1(new, turns=range(T + 2)):
                for j in turns:
                    a, b, c = j, j - 1, j - 2
                    if a == 0:
                        dve.wait_ge(xb_ready, at(new, T, T))
                        if new is not FIRST:
                            dve.wait_ge(x1b_ready, at(new, T, 0))
                    if a < T:
                        dve.wait_ge(p1_done, at(new, T, a + 1))
                        dve.reciprocal(inv_rows[:, a:a + 1], bank_b[a][:, F:F + 1]).then_inc(inv_ready, 1)
                    if 0 <= b < T:
                        dve.wait_ge(std1_ready, at(new, T, b + 1))
                        dve.reciprocal(rstd1[:, b:b + 1], std1[:, b:b + 1]).then_inc(rstd1_ready, 1)
                    if a < T:
                        dve.wait_ge(inv_ready, at(new, T, a + 1))
                        dve.scalar_tensor_tensor(v1[:, a, :], bank_b[a][:, 0:F], inv_rows[:, a:a + 1], xb[:, a, :],
                                                 ALU.mult, ALU.add).then_inc(v1_ready, 1)
                    if 0 <= b < T:
                        dve.wait_ge(rstd1_ready, at(new, T, b + 1))
                        dve.tensor_scalar(x1[:, b, :], v1[:, b, :], moments1[:, b, 0:1], rstd1[:, b:b + 1],
                                          ALU.subtract, ALU.mult).then_inc(x1_ready, 1)
                    if a < T:
                        dve.wait_ge(v1_ready, at(new, T, a + 1))
                        dve.bn_stats(stats1[:, a, :], v1[:, a, :]).then_inc(stats1_ready, 1)
                    if 0 <= c < T:
                        dve.wait_ge(x1_hi_ready, at(new, T, c + 1))
                        sub_hi(x1_lo[:, c, :], x1[:, c, :], x1_hi[:, c, :]).then_inc(x1_split, 1)
                    if a < T:
                        dve.wait_ge(eps_set, 1)
                        dve.wait_ge(stats1_ready, at(new, T, a + 1))
                        dve.bn_aggr(moments1[:, a, :], stats1[:, a, :]).then_inc(moments1_ready, 1)

            def g(new, f):
                dve.wait_ge(g_hi_ready, at(new, KF, f + 1))
                sub_hi(g_lo[:, f, :], bank_a[2 + f][:, :], g_hi[:, f, :]).then_inc(g_split, 1)

            def x2(new, f):
                dve.wait_ge(x2_hi_ready, at(new, KF, f + 1))
                sub_hi(x2_lo[:, f, :], relu[:, f, :], x2_hi[:, f, :]).then_inc(x2_split, 1)

            def x3(old, f):
                dve.wait_ge(x3_hi_ready, at(old, KF, f + 1))
                sub_hi(x3_lo[:, f, :], relu[:, f, :], x3_hi[:, f, :]).then_inc(x3_split, 1)

            def norm2(old, turns=range(T + 1)):
                for j in turns:
                    a, b = j, j - 1
                    if a == 0:
                        dve.wait_ge(x1b_ready, at(old, T, T))
                        dve.wait_ge(stored, at(old, DMA, DMA))
                    if a < T:
                        dve.wait_ge(p7_done, at(old, T, a + 1))
                        dve.tensor_tensor(v2[:, a, :], bank_b[a][:, 0:F], x1b[:, slot(old), a, :],
                                          ALU.add).then_inc(v2_ready, 1)
                    if b >= 0:
                        dve.wait_ge(std2_ready, at(old, T, b + 1))
                        dve.reciprocal(rstd2[:, b:b + 1], std2[:, b:b + 1]).then_inc(rstd2_ready, 1)
                    if a < T:
                        dve.wait_ge(v2_ready, at(old, T, a + 1))
                        dve.bn_stats(stats2[:, a, :], v2[:, a, :]).then_inc(stats2_ready, 1)
                    if b >= 0:
                        dve.wait_ge(rstd2_ready, at(old, T, b + 1))
                        dve.tensor_scalar(y[:, b, :], v2[:, b, :], moments2[:, b, 0:1], rstd2[:, b:b + 1],
                                          ALU.subtract, ALU.mult).then_inc(y_ready, 1)
                    if a < T:
                        dve.wait_ge(eps_set, 1)
                        dve.wait_ge(stats2_ready, at(old, T, a + 1))
                        dve.bn_aggr(moments2[:, a, :], stats2[:, a, :]).then_inc(moments2_ready, 1)

            def step(new, last=False):
                old, nxt = before(new), before(new, -1)
                if not last:
                    split_adj(nxt, 0)
                x3(old, 0)
                if not last:
                    split_adj(nxt, 1)
                    split_adj(nxt, 2)
                x3(old, 1)
                if not last:
                    split_adj(nxt, 3)
                g(new, 0)
                if not last:
                    split_xT(nxt, 0)
                    split_xT(nxt, 1)
                g(new, 1)
                s3(old)
                x2(new, 0)
                x2(new, 1)
                if not last:
                    norm2(old)
                    h(nxt)
                    s2(new)
                    norm1(nxt)

            dve.memset(eps_col[:, :], EPS).then_inc(eps_set, 1)
            for j in range(T):
                dve.memset(h_hi[:, j, F:F + ONES].bitcast(F32), 1.0).then_inc(ones_set, 1)
                dve.memset(h_lo[:, j, F:F + ONES].bitcast(F32), 0.0).then_inc(ones_set, 1)
            dve.wait_ge(w_loaded[0], DMA)
            dve.tensor_copy(w_hi[:, 0, :, :], w_raw[:, 0, :, :]).then_inc(w0_hi_ready, 1)
            dve.wait_ge(w0_hi_ready, 1)
            sub_hi(w_lo[:, 0, :, :], w_raw[:, 0, :, :], w_hi[:, 0, :, :]).then_inc(w0_split, 1)
            second = before(FIRST, -1)
            split_xT(FIRST, 0)
            split_xT(FIRST, 1)
            for k in range(T):
                split_adj(FIRST, k)
            h(FIRST)
            split_xT(second, 0)
            split_xT(second, 1)
            norm1(FIRST)
            split_w(1)
            h(second)
            for k in range(T):
                split_adj(second, k)
            g(FIRST, 0)
            g(FIRST, 1)
            split_w(2)
            norm1(second, range(0, 1))
            split_w(3)
            x2(FIRST, 0)
            x2(FIRST, 1)
            norm1(second, range(1, 2))
            s2(FIRST)
            norm1(second, range(2, T + 2))
            with dve.Fori(0, TURNS - 1) as turn:
                for r in range(1, RING + 1):
                    step((turn, r))
            for r in range(1, RING + 1):
                step((TURNS - 1, r), last=r == RING)
            norm2(before(LAST), range(0, 2))
            s2(LAST)
            norm2(before(LAST), range(2, 3))
            x3(LAST, 0)
            x3(LAST, 1)
            norm2(before(LAST), range(3, T + 1))
            s3(LAST)
            norm2(LAST)

        @block.gpsimd
        def _(pool):
            def add_b0(batch):
                pool.wait_ge(x_loaded, at(batch, DMA, DMA))
                for j in range(T):
                    if batch is not FIRST:
                        pool.wait_ge(v1_ready, at(batch, T, j + 1 - T))
                    pool.tensor_tensor(xb[:, j, :], x_raw[:, j, :], b0_all[:, :], ALU.add).then_inc(xb_ready, 1)

            def add_b3(batch):
                for j in range(T):
                    pool.wait_ge(x1_ready, at(batch, T, j + 1))
                    pool.tensor_tensor(x1b[:, slot(batch), j, :], x1[:, j, :], b3_all[:, :],
                                       ALU.add).then_inc(x1b_ready, 1)

            pool.wait_ge(b_loaded[0], DMA)
            add_b0(FIRST)
            pool.wait_ge(b_loaded[3], DMA)
            add_b3(FIRST)
            with pool.Fori(0, TURNS) as turn:
                for r in range(1, RING + 1):
                    add_b0((turn, r))
                    add_b3((turn, r))


def kernel(**inputs):
    import numpy as np
    import concourse.bacc as bacc
    from concourse.bass_utils import run_bass_kernel_spmd

    x = np.asarray(inputs["x"])
    adj = np.asarray(inputs["adj"])
    NB, N, F = x.shape
    T, KF = N // P, F // P
    arrays = {
        "xT": x.reshape(NB, P, T, KF, P).transpose(0, 4, 3, 2, 1).reshape(NB, P, KF, N),
        "x": x.reshape(NB, P, T, F),
        "adjT": adj.reshape(NB, P, T, P, T).transpose(0, 3, 4, 2, 1).reshape(NB, P, T, N),
    }
    for n, name in enumerate(("L0_gnn_W", "L1_gnn_W1", "L1_gnn_W2", "L1_gnn_W3")):
        arrays[f"w{n}"] = np.asarray(inputs[name]).reshape(KF, P, F).transpose(1, 0, 2)
    arrays["b0"] = np.asarray(inputs["L0_gnn_b"])
    arrays["b1"] = np.asarray(inputs["L1_gnn_b1"]).reshape(KF, P).T
    arrays["b2"] = np.asarray(inputs["L1_gnn_b2"]).reshape(KF, P).T
    arrays["b3"] = np.asarray(inputs["L1_gnn_b3"])
    arrays = {f"in_{k}": np.ascontiguousarray(a) for k, a in arrays.items()}

    nc = bacc.Bacc("TRN2", target_bir_lowering=False, num_devices=1)
    args = [nc.dram_tensor(k, a.shape, mybir.dt.from_np(a.dtype), kind="ExternalInput").ap()
            for k, a in arrays.items()]
    y = nc.dram_tensor("out_y", (NB, P, T, F), F32, kind="ExternalOutput").ap()
    build(nc, *args, y)
    r = run_bass_kernel_spmd(nc, [arrays], core_ids=[0])
    return r.results[0]["out_y"].reshape(NB, N, F)
```
